# Optimizing a Trainium2 kernel written in Bass

```python
import numpy as np
import jax
import jax.numpy as jnp

def _softmax(x, axis=-1):
    return jax.nn.softmax(x, axis=axis)

def _gelu(x):
    return jax.nn.gelu(x, approximate=True)

def _silu(x):
    return jax.nn.silu(x)

def _sigmoid(x):
    return jax.nn.sigmoid(x)

def _layernorm(x, axis=-1, eps=1e-05):
    m = jnp.mean(x, axis=axis, keepdims=True)
    v = jnp.var(x, axis=axis, keepdims=True)
    return (x - m) / jnp.sqrt(v + eps)

def _scatter_add(tgt, idx, src, axis=0):
    return tgt.at[idx].add(src)

def _segment_sum(src, seg, n):
    return jax.ops.segment_sum(src, seg, n)
kernel_name = 'mk_gnn_ffn_d1_gnn_r8_1d964c'

def setup_inputs(seed: int=0):
    np.random.seed(seed)
    _w = jnp.asarray

    def _rec_inputs():
        import jax
        import jax.numpy as jnp
        _gk = jax.random.key(seed)
        x = -0.000364 + 1 * jax.random.normal(jax.random.fold_in(_gk, 1), (1250, 768), jnp.float32)
        src = jax.random.randint(jax.random.fold_in(_gk, 2), (20000,), 0, 1250, jnp.int32)
        dst = jax.random.randint(jax.random.fold_in(_gk, 3), (20000,), 0, 1250, jnp.int32)
        _o = jnp.argsort(dst, stable=True)
        src = src[_o]
        dst = dst[_o]
        edge_type_4 = jax.random.randint(jax.random.fold_in(_gk, 12), (20000,), 0, 4, jnp.int32)
        return (x, src, dst, edge_type_4)
    x, src, dst, edge_type_4 = _rec_inputs()

    def _L0_gnn_setup():
        import jax, jax.numpy as jnp
        import numpy as np
        N_NODES = 2500
        N_EDGES = 12500
        D = 768
        NUM_REL = 4

        def _rgcn_conv(x, weight, root, bias, src, dst, etype):
            n = x.shape[0]
            out = x @ root + bias
            for r in range(NUM_REL):
                sel = etype == r
                self_f = sel.astype(x.dtype)
                deg = jnp.zeros((n,), x.dtype).at[dst].add(self_f)
                norm = jnp.where(sel, 1.0 / jnp.maximum(deg[dst], 1.0), 0.0)
                h_r = x @ weight[r]
                msgs = h_r[src] * norm[:, None]
                out = out + jax.ops.segment_sum(msgs, dst, num_segments=n)
            return out
        key = jax.random.key(seed)
        ks = jax.random.split(key, 12)
        entity = jax.random.normal(ks[0], (N_NODES, D), dtype=jnp.float32)
        edge_index = jax.random.randint(ks[1], (2, N_EDGES), 0, N_NODES, dtype=jnp.int64)
        edge_type = jax.random.randint(ks[2], (N_EDGES,), 0, NUM_REL, dtype=jnp.int64)
        s = 0.02
        params = {}
        for i, layer in enumerate(['1', '2', '3']):
            params[f'W{layer}'] = jax.random.normal(ks[3 + 3 * i], (NUM_REL, D, D), dtype=jnp.float32) * s
            params[f'root{layer}'] = jax.random.normal(ks[4 + 3 * i], (D, D), dtype=jnp.float32) * s
            params[f'b{layer}'] = jnp.zeros((D,), dtype=jnp.float32)
        return {'entity': entity, 'edge_index': edge_index, 'edge_type': edge_type, **params}
    _L0_gnn_all = _L0_gnn_setup()
    _L0_gnn_in = {k: v for k, v in _L0_gnn_all.items() if k in ('W1', 'root1', 'b1', 'W2', 'root2', 'b2', 'W3', 'root3', 'b3')}
    del _L0_gnn_all

    def _L0_ffn_setup():
        import jax, jax.numpy as jnp
        import numpy as np
        H = 768
        R = 64
        E = 8
        B, S = (8, 256)
        key = jax.random.key(seed)
        ks = jax.random.split(key, 10)
        s_in = 1.0 / np.sqrt(H)
        s_r = 1.0 / np.sqrt(R)
        return {'x': jax.random.normal(ks[0], (B, S, H), dtype=jnp.float32), 'enc_w': jax.random.uniform(ks[1], (H, R), jnp.float32, -s_in, s_in), 'enc_b': jax.random.uniform(ks[2], (R,), jnp.float32, -s_in, s_in), 'sw_w': jax.random.uniform(ks[3], (R, E), jnp.float32, -s_r, s_r), 'sw_b': jax.random.uniform(ks[4], (E,), jnp.float32, -s_r, s_r), 'w1': jax.random.uniform(ks[5], (E, H, R), jnp.float32, -s_in, s_in), 'b1': jax.random.uniform(ks[6], (E, R), jnp.float32, -s_in, s_in), 'w2': jax.random.uniform(ks[7], (E, R, H), jnp.float32, -s_r, s_r), 'b2': jax.random.uniform(ks[8], (E, H), jnp.float32, -s_r, s_r)}
    _L0_ffn_all = _L0_ffn_setup()
    _L0_ffn_in = {k: v for k, v in _L0_ffn_all.items() if k in ('enc_w', 'enc_b', 'sw_w', 'sw_b', 'w1', 'b1', 'w2', 'b2')}
    del _L0_ffn_all
    return {'x': x, 'src': src, 'dst': dst, 'edge_type_4': edge_type_4, 'L0_gnn_W1': _L0_gnn_in['W1'], 'L0_gnn_root1': _L0_gnn_in['root1'], 'L0_gnn_b1': _L0_gnn_in['b1'], 'L0_gnn_W2': _L0_gnn_in['W2'], 'L0_gnn_root2': _L0_gnn_in['root2'], 'L0_gnn_b2': _L0_gnn_in['b2'], 'L0_gnn_W3': _L0_gnn_in['W3'], 'L0_gnn_root3': _L0_gnn_in['root3'], 'L0_gnn_b3': _L0_gnn_in['b3'], 'L0_ffn_enc_w': _L0_ffn_in['enc_w'], 'L0_ffn_enc_b': _L0_ffn_in['enc_b'], 'L0_ffn_sw_w': _L0_ffn_in['sw_w'], 'L0_ffn_sw_b': _L0_ffn_in['sw_b'], 'L0_ffn_w1': _L0_ffn_in['w1'], 'L0_ffn_b1': _L0_ffn_in['b1'], 'L0_ffn_w2': _L0_ffn_in['w2'], 'L0_ffn_b2': _L0_ffn_in['b2']}

def reference(x, src, dst, edge_type_4, L0_gnn_W1, L0_gnn_root1, L0_gnn_b1, L0_gnn_W2, L0_gnn_root2, L0_gnn_b2, L0_gnn_W3, L0_gnn_root3, L0_gnn_b3, L0_ffn_enc_w, L0_ffn_enc_b, L0_ffn_sw_w, L0_ffn_sw_b, L0_ffn_w1, L0_ffn_b1, L0_ffn_w2, L0_ffn_b2):
    import jax
    import jax.numpy as jnp

    def _L0_gnn_ref(entity, edge_index, edge_type, W1, root1, b1, W2, root2, b2, W3, root3, b3):
        import jax, jax.numpy as jnp
        import numpy as np
        N_NODES = 2500
        N_EDGES = 12500
        D = 768
        NUM_REL = 4

        def _rgcn_conv(x, weight, root, bias, src, dst, etype):
            n = x.shape[0]
            out = x @ root + bias
            for r in range(NUM_REL):
                sel = etype == r
                self_f = sel.astype(x.dtype)
                deg = jnp.zeros((n,), x.dtype).at[dst].add(self_f)
                norm = jnp.where(sel, 1.0 / jnp.maximum(deg[dst], 1.0), 0.0)
                h_r = x @ weight[r]
                msgs = h_r[src] * norm[:, None]
                out = out + jax.ops.segment_sum(msgs, dst, num_segments=n)
            return out
        src, dst = (edge_index[0], edge_index[1])
        x = jax.nn.relu(_rgcn_conv(entity, W1, root1, b1, src, dst, edge_type))
        x = jax.nn.relu(_rgcn_conv(x, W2, root2, b2, src, dst, edge_type))
        x = _rgcn_conv(x, W3, root3, b3, src, dst, edge_type)
        return x

    def _L0_ffn_ref(x, enc_w, enc_b, sw_w, sw_b, w1, b1, w2, b2):
        import jax, jax.numpy as jnp
        import numpy as np
        H = 768
        R = 64
        E = 8
        B, S = (8, 256)
        b, s, d = x.shape
        xt = x.reshape(-1, d)
        x_enc = xt @ enc_w + enc_b
        route_prob = jax.nn.softmax(x_enc @ sw_w + sw_b, axis=-1)
        route_prob_max = jnp.max(route_prob, axis=-1)
        routes = jnp.argmax(route_prob, axis=-1)
        onehot = jax.nn.one_hot(routes, E, dtype=xt.dtype)
        h = jnp.einsum('td,edr->ter', xt, w1) + b1[None]
        h = jax.nn.gelu(h, approximate=False)
        h = h * onehot[..., None]
        out = jnp.einsum('ter,erd->td', h, w2) + onehot @ b2
        out = out * route_prob_max[:, None]
        return out.reshape(b, s, d)
    edge_index = jnp.stack([src, dst])
    x = x + _L0_gnn_ref(_layernorm(x, axis=-1), edge_index, edge_type_4, L0_gnn_W1, L0_gnn_root1, L0_gnn_b1, L0_gnn_W2, L0_gnn_root2, L0_gnn_b2, L0_gnn_W3, L0_gnn_root3, L0_gnn_b3)
    x = x + _L0_ffn_ref(_layernorm(x, axis=-1)[None], L0_ffn_enc_w, L0_ffn_enc_b, L0_ffn_sw_w, L0_ffn_sw_b, L0_ffn_w1, L0_ffn_b1, L0_ffn_w2, L0_ffn_b2)[0]
    return x

_drawn_inputs = setup_inputs


def setup_inputs(seed=0):
    import zlib

    import numpy as np

    out = dict(_drawn_inputs(seed))
    spreads = {'L0_gnn_b1': (0.0, 0.1), 'L0_gnn_b2': (0.0, 0.1), 'L0_gnn_b3': (0.0, 0.1)}
    factors = {'L0_ffn_enc_b': 8.0, 'L0_ffn_sw_b': 2.741, 'L0_ffn_b1': 39.952, 'L0_ffn_b2': 4.61}
    for name, (base, spread) in spreads.items():
        noise = np.random.default_rng([zlib.crc32(name.encode()), seed]).standard_normal(out[name].shape)
        drawn = base * np.exp(spread * noise) if base else spread * noise
        out[name] = jnp.asarray(drawn.astype(out[name].dtype))
    for name, factor in factors.items():
        out[name] = (out[name] * factor).astype(out[name].dtype)
    return out
```

```python
import concourse.bass as bass
from concourse import mybir
from contextlib import ExitStack

NODES = 1250
D = 768
EDGES = 20000
RELS = 4
LAYERS = 3
EXPERTS = 8
RANK = 64

ROWS = 125
TILES = NODES // ROWS
KD = D // 128
HALF = D // 2
PAIRS = 80
CHUNK = EDGES // (2 * PAIRS)
GROUP_DST = 25
GROUP = GROUP_DST * RELS
GROUPS = NODES // GROUP_DST
SRC_COLS = NODES + 4
CNT = TILES * NODES + 4
MATS = RELS + 1
X_TILES = 2 * MATS * TILES
G_TILES = 2 * RELS * TILES
T_TILES = 2 * TILES

XS = 16.0
WS = 1024.0
EPS = 1e-5


def gnn_ffn(nc, x, src, dst, etype, conv_w, conv_b, enc_w, enc_b, sw_w, sw_b, w1, b1, w2, b2, out):
    fp32, fp16, i32 = mybir.dt.float32, mybir.dt.float16, mybir.dt.int32
    ALU = mybir.AluOpType
    ACT = mybir.ActivationFunctionType
    AX = mybir.AxisListType
    ds = bass.ds

    ctx = ExitStack()
    with ctx:
        ctx.enter_context(nc.allow_non_contiguous_dma(reason="small constant loads"))

        def sb(name, shape, dt):
            return ctx.enter_context(nc.sbuf_tensor(name, shape, dt))

        def sem(name):
            return ctx.enter_context(nc.semaphore(name))

        counts_dram = nc.dram_tensor("counts_scratch", (RELS, 128, CNT), fp16, kind="Internal").ap()
        deg_dram = nc.dram_tensor("deg_scratch", (NODES * RELS,), fp32, kind="Internal").ap()

        counts = sb("counts", [128, RELS, CNT], fp16)
        xT = sb("xT", [128, 2, KD, TILES, 128], fp16)
        acc = sb("acc", [128, TILES, D], fp32)
        w_stage = sb("w_stage", [128, 2, KD, HALF], fp32)
        w_sb = sb("w_sb", [128, 2, 2, KD, HALF], fp16)
        bias = sb("bias", [128, D], fp32)
        stage = sb("stage", [128, 2, HALF], fp32)
        ident = sb("ident", [128, 128], fp32)
        key_t = sb("key_t", [128, 2, PAIRS], fp32)
        src_t = sb("src_t", [128, 2, PAIRS], fp32)
        inv_deg = sb("inv_deg", [128, TILES, RELS], fp32)
        group_lo = sb("group_lo", [128, GROUPS], fp32)
        pair_up = sb("pair_up", [128, 1], fp32)
        pair_down = sb("pair_down", [128, 1], fp32)
        key_min = sb("key_min", [128, 1], fp32)
        key_max = sb("key_max", [128, 1], fp32)
        meets = sb("meets", [128, 4, GROUPS], fp32)
        before = sb("before", [128, GROUPS + 1], fp32)
        ends = sb("ends", [128, 4], fp32)
        starts = sb("starts", [1, 2, GROUPS + 1], fp32)
        table = sb("table", [1, 2, GROUPS + 1], i32)
        stats = sb("stats", [128, TILES, 2, 6], fp32)
        mean_var = sb("mean_var", [128, TILES, 2], fp32)
        rstd = sb("rstd", [128, 4, TILES], fp32)
        enc_bs = sb("enc_bs", [128, 1], fp32)
        sw_ws = sb("sw_ws", [128, EXPERTS], fp32)
        sw_bs = sb("sw_bs", [128, 2, EXPERTS], fp32)
        b1s = sb("b1s", [128, EXPERTS // 2], fp32)
        descending = sb("descending", [128, EXPERTS], fp32)
        pick = sb("pick", [EXPERTS, EXPERTS // 2, 128], fp32)
        logits = sb("logits", [128, 2, EXPERTS], fp32)
        rank = sb("rank", [128, 2, EXPERTS], fp32)
        gate = sb("gate", [128, 2, EXPERTS], fp32)
        exps = sb("exps", [128, 2, EXPERTS], fp32)
        route = sb("route", [128, 5, 2], fp32)

        free = counts[:, 2:4, :].rearrange("p r n -> p (r n)")
        H_N = 2 * 2 * TILES * HALF
        h = free[:, 0:H_N].rearrange("p (a b t n) -> p a b t n", a=2, b=2, t=TILES)
        x_again = free[:, H_N:H_N + 4 * D].bitcast(fp32).rearrange("p (a n) -> p a n", a=2)
        edge_room = xT[:, 0, :, :, :].rearrange("p k t n -> p (k t n)").bitcast(fp32)
        PE_ = 2 * CHUNK
        edge_i = edge_room[0:PAIRS, 0:3 * PE_].bitcast(i32).rearrange("p (a n) -> p a n", a=3)
        key_f = edge_room[0:PAIRS, 3 * PE_:4 * PE_]
        src_f = edge_room[0:PAIRS, 4 * PE_:5 * PE_]
        hot_room = w_stage[:, 1, :, :].rearrange("p k n -> p (k n)").bitcast(fp16)
        hot_src = [hot_room[:, i * SRC_COLS:(i + 1) * SRC_COLS] for i in range(2)]
        iota_src = hot_room[:, 2 * SRC_COLS:3 * SRC_COLS]
        at = 3 * SRC_COLS
        hot_key = [hot_room[:, at + i * GROUP:at + (i + 1) * GROUP] for i in range(2)]
        iota_key = hot_room[:, at + 2 * GROUP:at + 3 * GROUP]
        ones = hot_room[:, at + 3 * GROUP:at + 3 * GROUP + 128]
        zeros = hot_room[:, at + 3 * GROUP + 128:at + 3 * GROUP + 256]
        assert at + 3 * GROUP + 256 <= 2 * KD * HALF
        deg_row = acc[0:1, :, :].rearrange("p t n -> p (t n)")[:, 0:NODES * RELS]
        stage_flat = w_stage[:, :, :, :].rearrange("p a k n -> p (a k n)")
        HID = EXPERTS * RANK
        KH = HID // 128
        w1_f = stage_flat[:, 0:KD * HID].rearrange("p (k n) -> p k n", k=KD)
        enc_f = stage_flat[:, KD * HID:KD * (HID + RANK)].rearrange("p (k n) -> p k n", k=KD)
        w_flat = w_sb[:, :, :, :, :].rearrange("p a b k n -> p (a b k n)")
        w1s = w_flat[:, 0:2 * KD * HID].rearrange("p (b k n) -> p b k n", b=2, k=KD)
        at = 2 * KD * HID
        encs = w_flat[:, at:at + 2 * KD * RANK].rearrange("p (b k n) -> p b k n", b=2, k=KD)
        at += 2 * KD * RANK
        b2s = w_flat[0:EXPERTS, at:at + 2 * D].bitcast(fp32)
        w2_f = counts[:, 0, 0:2 * KH * D].bitcast(fp32).rearrange("p (k n) -> p k n", k=KH)
        w2s = counts[:, 0, 2 * KH * D:4 * KH * D].rearrange("p (b k n) -> p b k n", b=2, k=KH)
        TOK = 256
        hid = free[:, 0:2 * KH * TOK].rearrange("p (b k n) -> p b k n", b=2, k=KH)
        at = 2 * KH * TOK
        gel = free[:, at:at + 2 * KH * TOK].bitcast(fp32).rearrange("p (k n) -> p k n", k=KH)
        at += 2 * KH * TOK
        gated = free[:, at:at + 2 * KH * TOK].bitcast(fp32).rearrange("p (k n) -> p k n", k=KH)
        at += 2 * KH * TOK
        x_enc = free[0:RANK, at:at + 2 * TOK].bitcast(fp32)
        at += 2 * TOK
        gate_t = free[0:EXPERTS, at:at + 2 * TOK].bitcast(fp32)
        assert at + 2 * TOK <= H_N

        bank = [ctx.enter_context(nc.psum_tensor(f"bank{i}", [128, 512], fp32)) for i in range(8)]
        x_bank, g_bank, t_bank = bank[0:2], bank[2:4], bank[6:8]

        edges_loaded = sem("edges_loaded")
        x_loaded = sem("x_loaded")
        consts_made = sem("consts_made")
        prep = sem("prep")
        prep_pe = sem("prep_pe")
        hot_ready = [sem("hot_ready_a"), sem("hot_ready_b")]
        hot_used = [sem("hot_used_a"), sem("hot_used_b")]
        group_counted = sem("group_counted")
        group_copied = sem("group_copied")
        counts_stored = sem("counts_stored")
        deg_stored = sem("deg_stored")
        deg_loaded = sem("deg_loaded")
        inv_made = sem("inv_made")
        counts_loaded = [sem("counts_loaded_0"), sem("counts_loaded_1")]
        w_loaded = [sem("w_loaded_0"), sem("w_loaded_1")]
        w_high = sem("w_high")
        w_ready = [sem("w_ready_0"), sem("w_ready_1")]
        bias_loaded = sem("bias_loaded")
        bias_scaled = sem("bias_scaled")
        ln_step = sem("ln_step")
        ln_root = sem("ln_root")
        staged = sem("staged")
        x_done = sem("x_done")
        h_high = sem("h_high")
        x_free = sem("x_free")
        g_done = sem("g_done")
        g_free = sem("g_free")
        t_done = sem("t_done")
        t_high = sem("t_high")
        t_free = sem("t_free")
        x_again_loaded = [sem("x_again_loaded_0"), sem("x_again_loaded_1")]
        residual = sem("residual")
        ffn_small = sem("ffn_small")
        ffn_w = sem("ffn_w")
        w2_loaded = sem("w2_loaded")
        b2_loaded = sem("b2_loaded")
        ffn_high = sem("ffn_high")
        ffn_ready = sem("ffn_ready")
        enc_done = sem("enc_done")
        enc_copied = sem("enc_copied")
        logits_done = sem("logits_done")
        route_step = sem("route_step")
        exp_done = sem("exp_done")
        gate_turned = sem("gate_turned")
        gate_copied = sem("gate_copied")
        hid_done = sem("hid_done")
        gelu_done = sem("gelu_done")
        spread_done = sem("spread_done")
        gated_done = sem("gated_done")
        gated_high = sem("gated_high")
        hid_ready = sem("hid_ready")
        out_done = sem("out_done")
        out_added = sem("out_added")
        out_stored = sem("out_stored")

        CONSTS = 13

        block = ctx.enter_context(nc.Block())

        @block.sync
        def _(sp):
            for i, a in enumerate((src, dst, etype)):
                sp.dma_start(edge_i[:, i, :], a.rearrange("(p n) -> p n", p=PAIRS)).then_inc(edges_loaded, 16)
            x_tiles = x.rearrange("(t p) d -> p t d", p=ROWS)
            sp.dma_start(acc[0:ROWS, :, :], x_tiles).then_inc(x_loaded, 16)

            def load_w(layer, m, half):
                mat = conv_w[ds(layer, 1), m, :, half * HALF:(half + 1) * HALF]
                sp.dma_start(w_stage[:, half, :, :],
                             mat.rearrange("a (k p) n -> p (a k) n", p=128)).then_inc(w_loaded[half], 16)

            def load_bias(layer):
                sp.dma_start(bias[0:ROWS, :], conv_b[ds(layer, 1), :].to_broadcast([ROWS, D]))\
                  .then_inc(bias_loaded, 16)

            load_w(0, 0, 0)
            load_bias(0)
            sp.dma_start(enc_bs[0:RANK, :], enc_b.rearrange("(p a) -> p a", a=1)).then_inc(ffn_small, 16)
            sp.dma_start(sw_ws[0:RANK, :], sw_w).then_inc(ffn_small, 16)
            for j in range(2):
                sp.dma_start(sw_bs[0:ROWS, j, :], sw_b.rearrange("(a e) -> a e", a=1).to_broadcast([ROWS, EXPERTS]))\
                  .then_inc(ffn_small, 16)
            sp.dma_start(b1s[:, :], b1.rearrange("(k a) r -> (a r) k", a=2)).then_inc(ffn_small, 16)

            sp.wait_ge(group_copied, 2 + GROUPS)
            load_w(0, 0, 1)
            sp.dma_start(deg_dram.rearrange("(a n) -> a n", a=1), deg_row).then_inc(deg_stored, 16)
            for r in (2, 3, 0, 1):
                sp.dma_start(counts_dram[r], counts[:, r, :]).then_inc(counts_stored, 16)
            sp.wait_ge(deg_stored, 16)
            sp.dma_start(inv_deg[0:ROWS, :, :], deg_dram.rearrange("(t p r) -> p t r", p=ROWS, r=RELS))\
              .then_inc(deg_loaded, 16)
            for half in range(2):
                sp.wait_ge(w_ready[half], 1)
                load_w(0, 1, half)
            sp.wait_ge(counts_stored, 16 * RELS)

            def next_w(layer, m, half):
                sp.wait_ge(w_ready[half], layer * MATS + m)
                load_w(layer, m, half)

            def load_counts(layer, r):
                sp.wait_ge(g_done, (layer * RELS + r - 1) * 2 * TILES)
                sp.dma_start(counts[:, r % 2, :], counts_dram[r]).then_inc(counts_loaded[r % 2], 16)

            def layer_loads(layer, last):
                for half in range(2):
                    next_w(layer, 2, half)
                if not last:
                    sp.wait_ge(x_free, 2 + layer * X_TILES + 2 * TILES)
                    load_bias(layer + 1)
                for half in range(2):
                    next_w(layer, 3, half)
                next_w(layer, 4, 0)
                load_counts(layer, 2)
                next_w(layer, 4, 1)
                if not last:
                    next_w(layer + 1, 0, 0)
                load_counts(layer, 3)
                if not last:
                    next_w(layer + 1, 0, 1)
                    next_w(layer + 1, 1, 0)
                    load_counts(layer + 1, 0)
                    next_w(layer + 1, 1, 1)
                    load_counts(layer + 1, 1)

            with sp.Fori(0, LAYERS - 1) as layer:
                layer_loads(layer, False)
            layer_loads(LAYERS - 1, True)

            for half in range(2):
                sp.wait_ge(w_ready[half], LAYERS * MATS)
            for e in range(EXPERTS):
                sp.dma_start(w1_f[:, :, e * RANK:(e + 1) * RANK],
                             w1[e].rearrange("(k p) r -> p k r", p=128)).then_inc(ffn_w, 16)
            sp.dma_start(enc_f, enc_w.rearrange("(k p) r -> p k r", p=128)).then_inc(ffn_w, 16)
            sp.wait_ge(x_done, LAYERS * X_TILES)
            sp.dma_start(b2s, b2).then_inc(b2_loaded, 16)
            sp.wait_ge(g_done, (LAYERS * RELS - 1) * 2 * TILES)
            sp.dma_start(w2_f, w2.rearrange("(k a) r n -> (a r) k n", a=2)).then_inc(w2_loaded, 16)

            def load_x_again(t, slot):
                sp.dma_start(x_again[0:ROWS, slot, :], x[ds(t * ROWS, ROWS), :])\
                  .then_inc(x_again_loaded[slot], 16)

            for j in range(2):
                load_x_again(j, j)
            with sp.Fori(1, TILES // 2) as tp:
                for j in range(2):
                    sp.wait_ge(residual, 2 * tp + j - 1)
                    load_x_again(2 * tp + j, j)
            with sp.Fori(0, TILES) as t:
                sp.wait_ge(out_added, 2 + 2 * t + 2)
                sp.dma_start(out[ds(t * ROWS, ROWS), :], acc[0:ROWS, ds(t, 1), :].rearrange("p a n -> p (a n)"))\
                  .then_inc(out_stored, 16)
            sp.wait_ge(out_stored, 16 * TILES)
            sp.wait_ge(deg_loaded, 16)

        @block.gpsimd
        def _(pool):
            pool.memset(ident[:, :], 0.0).then_inc(consts_made, 1)
            pool.memset(before[:, :], 1.0).then_inc(consts_made, 1)
            pool.memset(pick[:, :, :], 1.0).then_inc(consts_made, 1)
            pool.wait_ge(consts_made, 3)
            pool.affine_select(out=ident[:, :], in_=ident[:, :], compare_op=ALU.not_equal, fill=1.0,
                               base=0, pattern=[[-1, 128]], channel_multiplier=1).then_inc(consts_made, 1)
            pool.affine_select(out=before[:, :], in_=before[:, :], compare_op=ALU.is_gt, fill=0.0,
                               base=0, pattern=[[1, GROUPS + 1]], channel_multiplier=-1).then_inc(consts_made, 1)
            pick4 = pick[:, :, :].rearrange("e k (a r) -> e k a r", a=2)
            pool.affine_select(out=pick4, in_=pick4, compare_op=ALU.is_equal, fill=0.0, base=0,
                               pattern=[[-2, KH], [-1, 2], [0, RANK]], channel_multiplier=1)\
                .then_inc(consts_made, 1)
            pool.iota(group_lo[:, :], [[GROUP, GROUPS]], base=0, channel_multiplier=0,
                      allow_small_or_imprecise_dtypes=True).then_inc(consts_made, 1)
            pool.iota(pair_up[:, :], [[0, 1]], base=1, channel_multiplier=1,
                      allow_small_or_imprecise_dtypes=True).then_inc(consts_made, 1)
            pool.iota(pair_down[:, :], [[0, 1]], base=PAIRS, channel_multiplier=-1,
                      allow_small_or_imprecise_dtypes=True).then_inc(consts_made, 1)
            pool.iota(descending[:, :], [[-1, EXPERTS]], base=EXPERTS, channel_multiplier=0,
                      allow_small_or_imprecise_dtypes=True).then_inc(consts_made, 1)
            pool.iota(iota_src, [[1, SRC_COLS]], base=0, channel_multiplier=0,
                      allow_small_or_imprecise_dtypes=True).then_inc(consts_made, 1)
            pool.iota(iota_key, [[1, GROUP]], base=0, channel_multiplier=0,
                      allow_small_or_imprecise_dtypes=True).then_inc(consts_made, 1)
            pool.memset(ones, 1.0)
            pool.memset(zeros, 0.0)
            pool.memset(counts[:, :, TILES * NODES:CNT], 0.0)
            pool.wait_ge(prep_pe, 3)
            for part in range(2):
                pool.memset(xT[:, part, :, :, ROWS:128], 0.0)
            pool.drain().then_inc(consts_made, 1)

        @block.tensor
        def _(pe):
            pe.wait_ge(consts_made, 12)
            pe.wait_ge(prep, 2)
            for i, table_f in enumerate((key_f, src_f)):
                for c in range(2):
                    tr = pe.transpose(bank[6][0:CHUNK, (2 * i + c) * PAIRS:(2 * i + c + 1) * PAIRS],
                                      table_f[:, c * CHUNK:(c + 1) * CHUNK], ident[0:PAIRS, 0:PAIRS])
            tr.then_inc(prep_pe, 1)
            pe.wait_ge(prep, 7)
            pe.transpose(bank[7][0:GROUPS, 0:PAIRS], meets[0:PAIRS, 2, :], ident[0:PAIRS, 0:PAIRS])
            pe.transpose(bank[7][0:GROUPS, PAIRS:2 * PAIRS], meets[0:PAIRS, 3, :], ident[0:PAIRS, 0:PAIRS])\
              .then_inc(prep_pe, 1)
            pe.wait_ge(prep, 14)
            pe.matmul(bank[5][0:1, 0:GROUPS + 1], ends[0:GROUPS, 2:3], before[0:GROUPS, :], start=True, stop=True)
            pe.matmul(bank[5][0:1, 64:64 + GROUPS], ends[0:GROUPS, 1:2], ident[0:GROUPS, 0:GROUPS],
                      start=True, stop=True).then_inc(prep_pe, 1)

            def transpose_tile(j, parity, count):
                pe.wait_ge(t_free, count + 1)
                for k in range(KD // 2):
                    tr = pe.transpose(t_bank[parity][:, k * 128:k * 128 + ROWS],
                                      stage[0:ROWS, j, k * 128:(k + 1) * 128], ident[0:ROWS, 0:ROWS])
                tr.then_inc(t_done, 1)

            def transpose_normalised(first, turn):
                with pe.Fori(0, TILES) as t:
                    for j in range(2):
                        pe.wait_ge(staged, turn * T_TILES + 2 * t + j + 1)
                        transpose_tile(j, j, first + 2 * t + j)

            pe.wait_ge(prep, 18)
            transpose_normalised(0, 0)

            pe.wait_ge(consts_made, CONSTS)
            with pe.Fori(0, GROUPS // 2) as gp:
                for j in range(2):
                    g = 2 * gp + j
                    left, right, deg = bank[3 * j], bank[3 * j + 1], bank[3 * j + 2]
                    pe.wait_ge(group_copied, g + 1)
                    for b in (left, right, deg):
                        pe.matmul(b[:, 0:1], zeros, zeros[:, 0:1], start=True, stop=False, skip_group_check=True)
                    first = pe.value_load(table[0:1, 0, ds(g, 1)], min_val=1, max_val=GROUPS * PAIRS)
                    last = pe.value_load(table[0:1, 0, ds(g + 1, 1)], min_val=2, max_val=GROUPS * PAIRS + 1)
                    with pe.Fori(first, last) as step:
                        for c in range(2):
                            pe.wait_ge(hot_ready[c], step)
                            for s in range(TILES):
                                b = left if s < TILES // 2 else right
                                o = s % (TILES // 2) * GROUP
                                pe.matmul(b[:, o:o + GROUP], hot_src[c][0:CHUNK, s * ROWS:s * ROWS + 128],
                                          hot_key[c][0:CHUNK, :], start=False, stop=False, skip_group_check=True)
                            pe.matmul(deg[:, 0:GROUP], ones[0:CHUNK, :], hot_key[c][0:CHUNK, :],
                                      start=False, stop=False, skip_group_check=True).then_inc(hot_used[c], 1)
                    pe.matmul(deg[:, 0:1], zeros, zeros[:, 0:1], start=False, stop=True,
                              skip_group_check=True).then_inc(group_counted, 1)

            def product_x(layer, u):
                half = u % 2
                with pe.Fori(0, TILES // 2) as tp:
                    pe.wait_ge(w_ready[half], layer * MATS + u // 2 + 1)
                    if u == 0:
                        pe.wait_ge(t_free, 2 + (layer + 1) * T_TILES)
                    for j in range(2):
                        t = 2 * tp + j
                        n = layer * X_TILES + u * TILES + t
                        pe.wait_ge(x_free, n + 1)
                        for k in range(KD):
                            for a, b in ((0, 0), (0, 1), (1, 0)):
                                mm = pe.matmul(x_bank[j][:, 0:HALF],
                                               xT[:, a, k, ds(t, 1), :].rearrange("p a n -> p (a n)"),
                                               w_sb[:, half, b, k, :],
                                               start=(k == 0 and a == 0 and b == 0),
                                               stop=(k == KD - 1 and a == 1))
                        mm.then_inc(x_done, 1)

            def counts_tile(layer, r, half, t, parity):
                n = layer * G_TILES + (2 * r + half) * TILES + t
                pe.wait_ge(g_free, n + 1)
                for s in range(TILES):
                    lhs = counts[0:ROWS, r % 2, ds(s * NODES + t * ROWS, 128)]
                    for b in range(2):
                        mm = pe.matmul(g_bank[parity][:, 0:HALF], lhs, h[0:ROWS, half, b, s, :],
                                       start=(s == 0 and b == 0), stop=(s == TILES - 1 and b == 1))
                mm.then_inc(g_done, 1)

            def wait_product_g(layer, r, half):
                pe.wait_ge(x_free, 2 + layer * X_TILES + (2 * r + half + 3) * TILES)
                if half == 0:
                    pe.wait_ge(counts_loaded[r % 2], 16 * (2 * layer + r // 2 + 1))

            def product_g(layer, r, half):
                with pe.Fori(0, TILES // 2) as tp:
                    wait_product_g(layer, r, half)
                    for j in range(2):
                        counts_tile(layer, r, half, 2 * tp + j, j)

            def product_g_last(layer, half):
                r = RELS - 1
                wait_product_g(layer, r, half)

                def turn(t, parity):
                    pe.wait_ge(g_free, 2 + layer * G_TILES + (2 * r + half) * TILES + t + 1)
                    transpose_tile(parity, parity, (layer + 1) * T_TILES + half * TILES + t)

                counts_tile(layer, r, half, 0, 0)
                with pe.Fori(0, TILES // 2 - 1) as tp:
                    for t, parity in ((2 * tp + 1, 1), (2 * tp + 2, 0)):
                        counts_tile(layer, r, half, t, parity)
                        turn(t - 1, 1 - parity)
                counts_tile(layer, r, half, TILES - 1, 1)
                turn(TILES - 2, 0)
                turn(TILES - 1, 1)

            def layer_products(layer, last):
                for u in range(4):
                    product_x(layer, u)
                for r in range(RELS - 1):
                    for half in range(2):
                        product_g(layer, r, half)
                        product_x(layer, 2 * r + 4 + half)
                for half in range(2):
                    if last:
                        product_g(layer, RELS - 1, half)
                    else:
                        product_g_last(layer, half)

            pe.wait_ge(group_copied, 2 + GROUPS)
            with pe.Fori(0, LAYERS - 1) as layer:
                layer_products(layer, False)
            layer_products(LAYERS - 1, True)

            transpose_normalised(LAYERS * T_TILES, 1)
            pe.wait_ge(ffn_ready, 3)
            pe.wait_ge(ffn_small, 80)

            def tokens(part, k, c):
                return xT[:, part, k, ds(2 * c, 2), :].rearrange("p a n -> p (a n)")

            def three(bank_ap, weights, cols, c):
                for k in range(KD):
                    for a, b in ((0, 0), (1, 0), (0, 1)):
                        mm = pe.matmul(bank_ap, weights[:, a, k, cols], tokens(b, k, c),
                                       start=(k == 0 and a == 0 and b == 0), stop=(k == KD - 1 and b == 1))
                return mm

            def encode(c):
                three(bank[0][0:RANK, 0:TOK], encs, slice(0, RANK), c).then_inc(enc_done, 1)

            def hidden(c, k):
                pe.wait_ge(gelu_done, KH * c + k - 1) if k >= 2 or not isinstance(c, int) or c > 0 else None
                three(bank[2 + k % 2][:, 0:TOK], w1s, slice(k * 128, (k + 1) * 128), c).then_inc(hid_done, 1)

            def route_logits(c):
                pe.wait_ge(enc_copied, c + 1)
                for j in range(2):
                    mm = pe.matmul(bank[1][0:ROWS, j * EXPERTS:(j + 1) * EXPERTS],
                                   x_enc[:, j * 128:j * 128 + ROWS], sw_ws[0:RANK, :], start=True, stop=True)
                mm.then_inc(logits_done, 1)

            def turn_gates(c):
                pe.wait_ge(route_step, 7 * (c + 1))
                for j in range(2):
                    tr = pe.transpose(bank[1][0:EXPERTS, 64 + j * 128:64 + j * 128 + ROWS],
                                      gate[0:ROWS, j, :], ident[0:ROWS, 0:ROWS])
                tr.then_inc(gate_turned, 1)

            def spread_gates(c):
                pe.wait_ge(gate_copied, c + 1)
                for k in range(KH):
                    pe.matmul(bank[4 + k // 2][:, k % 2 * TOK:(k % 2 + 1) * TOK], pick[:, k, :],
                              gate_t, start=True, stop=True).then_inc(spread_done, 1)

            def outputs(c):
                pe.wait_ge(hid_ready, KH * (c + 1))
                for j in range(2):
                    for half in range(2):
                        n = 4 * c + 2 * j + half
                        pe.wait_ge(out_added, n + 1)
                        cols = slice(half * HALF, (half + 1) * HALF)
                        rows = slice(j * 128, j * 128 + ROWS)
                        ob = bank[6 + half][0:ROWS, 0:HALF]
                        for k in range(KH):
                            for a, b in ((0, 0), (0, 1), (1, 0)):
                                pe.matmul(ob, hid[:, a, k, rows], w2s[:, b, k, cols],
                                          start=(k == 0 and a == 0 and b == 0), stop=False)
                        pe.matmul(ob, gate_t[:, rows], b2s[:, cols], start=False, stop=True)\
                          .then_inc(out_done, 1)

            def tokens_front(c, first):
                encode(c)
                hidden(c, 0)
                route_logits(c)
                for k in range(1, KH):
                    hidden(c, k)
                if not first:
                    outputs(c - 1)
                turn_gates(c)
                spread_gates(c)

            tokens_front(0, True)
            with pe.Fori(1, TILES // 2) as c:
                tokens_front(c, False)
            outputs(TILES // 2 - 1)

        @block.vector
        def _(dve):
            for c in range(2):
                dve.sem_inc(hot_used[c], 1)
            dve.sem_inc(x_free, 2)
            dve.sem_inc(g_free, 2)
            dve.sem_inc(t_free, 2)
            dve.sem_inc(out_added, 2)
            for s in range(2):
                dve.sem_inc(counts_loaded[s], 16)

            dve.wait_ge(edges_loaded, 48)
            dve.scalar_tensor_tensor(key_f, edge_i[:, 1, :], float(RELS), edge_i[:, 2, :],
                                     ALU.mult, ALU.add).then_inc(prep, 1)
            dve.tensor_copy(src_f, edge_i[:, 0, :]).then_inc(prep, 1)
            dve.wait_ge(prep, 1)
            dve.tensor_reduce(key_min[0:PAIRS, :], key_f, AX.X, ALU.min).then_inc(prep, 1)
            dve.tensor_reduce(key_max[0:PAIRS, :], key_f, AX.X, ALU.max).then_inc(prep, 1)
            dve.wait_ge(prep, 4)
            dve.wait_ge(consts_made, 12)
            lo = group_lo[0:PAIRS, :]
            dve.tensor_scalar(meets[0:PAIRS, 0, :], lo, float(GROUP - 1), key_min[0:PAIRS, :],
                              ALU.add, ALU.is_ge).then_inc(prep, 1)
            dve.wait_ge(prep, 5)
            dve.scalar_tensor_tensor(meets[0:PAIRS, 1, :], lo, key_max[0:PAIRS, :], meets[0:PAIRS, 0, :],
                                     ALU.is_le, ALU.mult).then_inc(prep, 1)
            dve.wait_ge(prep, 6)
            dve.tensor_scalar(meets[0:PAIRS, 2, :], meets[0:PAIRS, 1, :], pair_up[0:PAIRS, :], None, ALU.mult)
            dve.tensor_scalar(meets[0:PAIRS, 3, :], meets[0:PAIRS, 1, :], pair_down[0:PAIRS, :], None,
                              ALU.mult).then_inc(prep, 1)
            dve.wait_ge(prep_pe, 1)
            dve.tensor_copy(key_t[0:CHUNK, :, :], bank[6][0:CHUNK, 0:2 * PAIRS].rearrange("p (c n) -> p c n", c=2))\
               .then_inc(prep, 1)
            dve.tensor_copy(src_t[0:CHUNK, :, :],
                            bank[6][0:CHUNK, 2 * PAIRS:4 * PAIRS].rearrange("p (c n) -> p c n", c=2))\
               .then_inc(prep, 1)
            dve.wait_ge(prep_pe, 2)
            G = slice(0, GROUPS)
            dve.tensor_reduce(ends[G, 0:2], bank[7][G, 0:2 * PAIRS].rearrange("p (a n) -> p a n", a=2),
                              AX.X, ALU.max).then_inc(prep, 1)
            dve.wait_ge(prep, 10)
            dve.tensor_scalar(ends[G, 0:1], ends[G, 0:1], 1.0, None, ALU.max).then_inc(prep, 1)
            dve.tensor_scalar(ends[G, 1:2], ends[G, 1:2], -1.0, float(PAIRS), ALU.mult, ALU.add).then_inc(prep, 1)
            dve.wait_ge(prep, 12)
            dve.tensor_scalar(ends[G, 3:4], ends[G, 0:1], -1.0, None, ALU.add).then_inc(prep, 1)
            dve.wait_ge(prep, 13)
            dve.tensor_tensor(ends[G, 1:2], ends[G, 1:2], ends[G, 3:4], ALU.min)
            dve.drain()
            dve.tensor_tensor(ends[G, 2:3], ends[G, 0:1], ends[G, 1:2], ALU.subtract).then_inc(prep, 1)
            dve.wait_ge(prep_pe, 3)
            dve.tensor_scalar(starts[:, 0, :], bank[5][0:1, 0:GROUPS + 1], 1.0, None, ALU.add).then_inc(prep, 1)
            dve.wait_ge(prep, 15)
            dve.tensor_tensor(starts[:, 1, G], bank[5][0:1, 64:64 + GROUPS], starts[:, 0, G],
                              ALU.subtract).then_inc(prep, 1)
            dve.tensor_copy(table[:, 0, :], starts[:, 0, :]).then_inc(prep, 1)
            dve.wait_ge(prep, 16)
            dve.tensor_copy(table[:, 1, G], starts[:, 1, G]).then_inc(prep, 1)

            R = slice(0, ROWS)

            def statistics(t):
                tile = acc[R, ds(t, 1), :].rearrange("p a (b n) -> p (a b) n", b=2)
                for b in range(2):
                    dve.bn_stats(stats[R, ds(t, 1), b, :].rearrange("p a n -> p (a n)"), tile[:, b, :])\
                       .then_inc(ln_step, 1)

            PER_TILE, TAIL = 3, 8
            NORM = PER_TILE * TILES + TAIL

            def aggregate(first):
                dve.wait_ge(ln_step, first + 2 * TILES)
                for t in range(TILES):
                    dve.bn_aggr(mean_var[R, t, :], stats[R, t, :, :].rearrange("p b n -> p (b n)"))\
                       .then_inc(ln_step, 1)

            def reciprocal_root(first, turn):
                n = first + PER_TILE * TILES

                def step(ins):
                    nonlocal n
                    ins.then_inc(ln_step, 1)
                    n += 1
                    dve.wait_ge(ln_step, n)

                var, root, tmp, inv = (rstd[R, i, :] for i in range(4))
                dve.wait_ge(ln_step, n)
                step(dve.tensor_scalar(var, mean_var[R, :, 1], EPS, None, ALU.add))
                dve.wait_ge(ln_root, turn)
                step(dve.reciprocal(inv, root))
                step(dve.tensor_tensor(tmp, inv, inv, ALU.mult))
                step(dve.tensor_tensor(tmp, tmp, var, ALU.mult))
                step(dve.tensor_scalar(tmp, tmp, -0.5, 1.5, ALU.mult, ALU.add))
                step(dve.tensor_tensor(inv, inv, tmp, ALU.mult))
                step(dve.tensor_scalar(inv, inv, XS, None, ALU.mult))
                step(dve.tensor_copy(tmp, inv))

            def low_of_tile(half, t, parity, count, op, scalar):
                dve.wait_ge(t_high, count + 1)
                ks = slice(half * KD // 2, (half + 1) * KD // 2)
                hi, lo_ = (xT[:, a, ks, ds(t, 1), 0:ROWS].rearrange("p k a n -> p k (a n)") for a in range(2))
                dve.scalar_tensor_tensor(lo_, t_bank[parity][:, 0:HALF].rearrange("p (k n) -> p k n", n=128)[:, :, 0:ROWS],
                                         scalar, hi, op, ALU.subtract).then_inc(t_free, 1)

            def normalise(first):
                with dve.Fori(0, TILES) as t:
                    for j in range(2):
                        dve.tensor_scalar(stage[R, j, :],
                                          acc[R, ds(t, 1), j * HALF:(j + 1) * HALF].rearrange("p a n -> p (a n)"),
                                          mean_var[R, ds(t, 1), 0], rstd[R, 3, ds(t, 1)],
                                          ALU.subtract, ALU.mult).then_inc(staged, 1)
                    for j in range(2):
                        low_of_tile(j, t, j, first + 2 * t + j, ALU.mult, 1.0)

            dve.wait_ge(x_loaded, 16)
            with dve.Fori(0, TILES) as t:
                statistics(t)
            aggregate(0)
            reciprocal_root(0, 1)
            normalise(0)

            dve.wait_ge(consts_made, CONSTS)
            with dve.Fori(0, GROUPS) as g:
                first = dve.value_load(table[0:1, 0, ds(g, 1)], min_val=1, max_val=GROUPS * PAIRS)
                last = dve.value_load(table[0:1, 0, ds(g + 1, 1)], min_val=2, max_val=GROUPS * PAIRS + 1)
                shift = dve.value_load(table[0:1, 1, ds(g, 1)], min_val=-GROUPS * PAIRS, max_val=PAIRS)
                with dve.Fori(first, last) as step:
                    pair = dve.snap(step + shift).with_bounds(min_val=0, max_val=PAIRS - 1)
                    for c in range(2):
                        dve.wait_ge(hot_used[c], step)
                        dve.tensor_scalar(hot_key[c][0:CHUNK, :], iota_key[0:CHUNK, :],
                                          group_lo[0:CHUNK, ds(g, 1)], key_t[0:CHUNK, c, ds(pair, 1)],
                                          ALU.add, ALU.is_equal)
                        dve.tensor_scalar(hot_src[c][0:CHUNK, :], iota_src[0:CHUNK, :],
                                          src_t[0:CHUNK, c, ds(pair, 1)], None,
                                          ALU.is_equal).then_inc(hot_ready[c], 1)

            def low_of_weights(layer, u):
                half = u % 2
                dve.wait_ge(w_high, layer * 2 * MATS + u + 1)
                dve.scalar_tensor_tensor(w_sb[:, half, 1, :, :], w_stage[:, half, :, :], WS,
                                         w_sb[:, half, 0, :, :], ALU.mult, ALU.subtract)\
                   .then_inc(w_ready[half], 1)

            low_of_weights(0, 0)
            low_of_weights(0, 1)
            dve.wait_ge(deg_stored, 16)

            DOWN = 1.0 / WS

            def add_bias(layer, half):
                with dve.Fori(0, TILES // 2) as tp:
                    dve.wait_ge(bias_scaled, layer + 1)
                    for j in range(2):
                        t = 2 * tp + j
                        dve.wait_ge(x_done, layer * X_TILES + half * TILES + t + 1)
                        cols = slice(half * HALF, (half + 1) * HALF)
                        dve.scalar_tensor_tensor(acc[R, ds(t, 1), cols].rearrange("p a n -> p (a n)"),
                                                 x_bank[j][R, 0:HALF], DOWN, bias[R, cols],
                                                 ALU.mult, ALU.add).then_inc(x_free, 1)

            def low_of_hidden(layer, u):
                half = u % 2
                with dve.Fori(0, TILES // 2) as tp:
                    for j in range(2):
                        t = 2 * tp + j
                        dve.wait_ge(h_high, layer * G_TILES + (u - 2) * TILES + t + 1)
                        hi, lo_ = (h[R, half, a, ds(t, 1), :].rearrange("p a n -> p (a n)") for a in range(2))
                        dve.scalar_tensor_tensor(lo_, x_bank[j][R, 0:HALF], DOWN, hi,
                                                 ALU.mult, ALU.subtract).then_inc(x_free, 1)

            def add_messages(layer, r, half, t, parity, target):
                n = layer * G_TILES + (2 * r + half) * TILES + t
                dve.wait_ge(g_done, n + 1)
                if isinstance(r, int) and r == 0:
                    dve.wait_ge(x_free, 2 + layer * X_TILES + (half + 1) * TILES)
                else:
                    dve.wait_ge(g_free, 2 + n - 2 * TILES + 1)
                cols = slice(half * HALF, (half + 1) * HALF)
                tile = acc[R, ds(t, 1), cols].rearrange("p a n -> p (a n)")
                dve.scalar_tensor_tensor(tile if target is None else target, g_bank[parity][R, 0:HALF],
                                         inv_deg[R, ds(t, 1), r], tile,
                                         ALU.mult, ALU.add).then_inc(g_free, 1)

            def add_relation(layer, r, half):
                with dve.Fori(0, TILES // 2) as tp:
                    for j in range(2):
                        add_messages(layer, r, half, 2 * tp + j, j, None)

            def add_last_relation(layer, half):
                r = RELS - 1

                def add(t, parity):
                    add_messages(layer, r, half, t, parity, stage[R, parity, :])

                def turn(t, parity):
                    low_of_tile(half, t, parity, (layer + 1) * T_TILES + half * TILES + t, ALU.max, 0.0)

                add(0, 0)
                with dve.Fori(0, TILES // 2 - 1) as tp:
                    for t, parity in ((2 * tp + 1, 1), (2 * tp + 2, 0)):
                        add(t, parity)
                        turn(t - 1, 1 - parity)
                add(TILES - 1, 1)
                turn(TILES - 2, 0)
                turn(TILES - 1, 1)

            def layer_work(layer, last):
                dve.wait_ge(bias_loaded, 16 * (layer + 1))
                dve.tensor_scalar(bias[R, :], bias[R, :], XS, None, ALU.mult).then_inc(bias_scaled, 1)
                for u in range(2):
                    add_bias(layer, u)
                    low_of_weights(layer, u + 2)
                for u in range(2, 4):
                    low_of_hidden(layer, u)
                    low_of_weights(layer, u + 2)
                for r in range(RELS - 1):
                    for half in range(2):
                        u = 2 * r + 4 + half
                        add_relation(layer, r, half)
                        low_of_hidden(layer, u)
                        if u + 2 < 2 * MATS or not last:
                            low_of_weights(layer, u + 2)
                for half in range(2):
                    if last:
                        add_relation(layer, RELS - 1, half)
                    else:
                        add_last_relation(layer, half)

            dve.wait_ge(deg_loaded, 16)
            dve.tensor_scalar(inv_deg[R, :, :], inv_deg[R, :, :], 1.0, None, ALU.max).then_inc(inv_made, 1)
            dve.wait_ge(inv_made, 1)
            dve.reciprocal(inv_deg[R, :, :], inv_deg[R, :, :]).then_inc(inv_made, 1)
            dve.wait_ge(inv_made, 2)
            with dve.Fori(0, LAYERS - 1) as layer:
                layer_work(layer, False)
            layer_work(LAYERS - 1, True)

            dve.wait_ge(ffn_high, 1)
            dve.scalar_tensor_tensor(w1s[:, 1, :, :], w1_f, WS, w1s[:, 0, :, :], ALU.mult, ALU.subtract)
            dve.scalar_tensor_tensor(encs[:, 1, :, :], enc_f, WS, encs[:, 0, :, :], ALU.mult,
                                     ALU.subtract).then_inc(ffn_ready, 1)
            dve.wait_ge(ffn_high, 2)
            dve.scalar_tensor_tensor(w2s[:, 1, :, :], w2_f, WS, w2s[:, 0, :, :], ALU.mult,
                                     ALU.subtract).then_inc(ffn_ready, 1)
            dve.wait_ge(b2_loaded, 16)
            dve.tensor_scalar(b2s, b2s, XS * WS, None, ALU.mult).then_inc(ffn_ready, 1)

            def add_x(tp, slot):
                t = 2 * tp + slot
                dve.wait_ge(x_again_loaded[slot], 16 * (tp + 1))
                dve.wait_ge(g_free, 2 + LAYERS * G_TILES)
                tile = acc[R, ds(t, 1), :].rearrange("p a n -> p (a n)")
                dve.scalar_tensor_tensor(tile, tile, 1.0 / XS, x_again[R, slot, :], ALU.mult,
                                         ALU.add).then_inc(residual, 1)

            with dve.Fori(0, TILES // 2) as tp:
                for j in range(2):
                    t = 2 * tp + j
                    add_x(tp, j)
                    dve.wait_ge(residual, t + 1)
                    statistics(t)
            aggregate(NORM)
            reciprocal_root(NORM, 2)
            normalise(LAYERS * T_TILES)

            largest, minus, total, prob, best = range(5)
            dve.wait_ge(g_done, LAYERS * G_TILES)
            dve.memset(gate_t, 0.0)

            def token_routes(c):
                n = 7 * c
                dve.wait_ge(enc_done, c + 1)
                dve.tensor_scalar(x_enc, bank[0][0:RANK, 0:TOK], 1.0 / (XS * WS), enc_bs[0:RANK, :],
                                  ALU.mult, ALU.add).then_inc(enc_copied, 1)
                dve.wait_ge(logits_done, c + 1)
                dve.tensor_tensor(logits[R, :, :], bank[1][R, 0:2 * EXPERTS].rearrange("p (j e) -> p j e", j=2),
                                  sw_bs[R, :, :], ALU.add).then_inc(route_step, 1)
                dve.wait_ge(route_step, n + 1)
                dve.tensor_reduce(route[R, largest, :], logits[R, :, :], AX.X, ALU.max).then_inc(route_step, 1)
                dve.wait_ge(route_step, n + 2)
                dve.tensor_scalar(route[R, minus, :], route[R, largest, :], -1.0, None, ALU.mult)\
                   .then_inc(route_step, 1)
                for j in range(2):
                    ins = dve.scalar_tensor_tensor(rank[R, j, :], logits[R, j, :], route[R, largest, j:j + 1],
                                                   descending[R, :], ALU.is_equal, ALU.mult)
                ins.then_inc(route_step, 1)
                dve.wait_ge(route_step, n + 4)
                dve.tensor_reduce(route[R, best, :], rank[R, :, :], AX.X, ALU.max).then_inc(route_step, 1)
                dve.wait_ge(exp_done, 2 * (c + 1))
                dve.reciprocal(route[R, prob, :], route[R, total, :]).then_inc(route_step, 1)
                dve.wait_ge(route_step, n + 6)
                for j in range(2):
                    ins = dve.tensor_scalar(gate[R, j, :], rank[R, j, :], route[R, best, j:j + 1],
                                            route[R, prob, j:j + 1], ALU.is_equal, ALU.mult)
                ins.then_inc(route_step, 1)

            def token_gates(c):
                dve.wait_ge(gate_turned, c + 1)
                dve.tensor_copy(gate_t.rearrange("e (j n) -> e j n", j=2)[:, :, 0:ROWS],
                                bank[1][0:EXPERTS, 64:64 + 2 * 128].rearrange("e (j n) -> e j n", j=2)[:, :, 0:ROWS])\
                   .then_inc(gate_copied, 1)
                for k in range(KH):
                    dve.wait_ge(spread_done, KH * c + (k | 1) + 1)
                    dve.wait_ge(gelu_done, KH * c + k + 1)
                    dve.tensor_tensor(gated[:, k, :], gel[:, k, :], bank[4 + k // 2][:, k % 2 * TOK:(k % 2 + 1) * TOK],
                                      ALU.mult).then_inc(gated_done, 1)
                for k in range(KH):
                    dve.wait_ge(gated_high, KH * c + k + 1)
                    dve.scalar_tensor_tensor(hid[:, 1, k, :], gated[:, k, :], XS, hid[:, 0, k, :],
                                             ALU.mult, ALU.subtract).then_inc(hid_ready, 1)

            def token_outputs(c):
                for j in range(2):
                    for half in range(2):
                        dve.wait_ge(out_done, 4 * c + 2 * j + half + 1)
                        tile = acc[R, ds(2 * c + j, 1), half * HALF:(half + 1) * HALF].rearrange("p a n -> p (a n)")
                        dve.scalar_tensor_tensor(tile, bank[6 + half][R, 0:HALF], 1.0 / (XS * WS), tile,
                                                 ALU.mult, ALU.add).then_inc(out_added, 1)

            token_routes(0)
            token_gates(0)
            with dve.Fori(1, TILES // 2) as c:
                token_routes(c)
                token_outputs(c - 1)
                token_gates(c)
            token_outputs(TILES // 2 - 1)

        @block.scalar
        def _(act):
            R = slice(0, ROWS)

            def high_of_tile(half, t, parity, count, func):
                act.wait_ge(t_done, count + 1)
                ks = slice(half * KD // 2, (half + 1) * KD // 2)
                act.activation(xT[:, 0, ks, ds(t, 1), 0:ROWS].rearrange("p k a n -> p k (a n)"),
                               t_bank[parity][:, 0:HALF].rearrange("p (k n) -> p k n", n=128)[:, :, 0:ROWS],
                               func).then_inc(t_high, 1)

            def high_of_normalised(first):
                with act.Fori(0, TILES) as t:
                    for j in range(2):
                        high_of_tile(j, t, j, first + 2 * t + j, ACT.Copy)

            PER_TILE, TAIL = 3, 8
            NORM = PER_TILE * TILES + TAIL

            def root(first):
                act.wait_ge(ln_step, first + PER_TILE * TILES + 1)
                act.activation(rstd[R, 1, :], rstd[R, 0, :], ACT.Sqrt).then_inc(ln_root, 1)

            act.sem_inc(group_copied, 2)
            root(0)
            act.wait_ge(prep_pe, 3)
            act.wait_ge(consts_made, CONSTS)
            high_of_normalised(0)

            by_relation = counts[:, :, 0:TILES * NODES].rearrange("p r (s n) -> p s r n", s=TILES)
            act.wait_ge(staged, T_TILES)
            with act.Fori(0, GROUPS // 2) as gp:
                for j in range(2):
                    g = 2 * gp + j
                    act.wait_ge(group_counted, g + 1)
                    for b in range(2):
                        ss = slice(b * TILES // 2, (b + 1) * TILES // 2)
                        act.activation(by_relation[:, ss, :, ds(g * GROUP_DST, GROUP_DST)],
                                       bank[3 * j + b][:, 0:GROUP * TILES // 2]
                                       .rearrange("p (s d r) -> p s r d", d=GROUP_DST, r=RELS), ACT.Copy)
                    act.activation(deg_row[:, ds(g * GROUP, GROUP)], bank[3 * j + 2][0:1, 0:GROUP], ACT.Copy)\
                       .then_inc(group_copied, 1)

            def high_of_weights(layer, u):
                half = u % 2
                act.wait_ge(w_loaded[half], 16 * (layer * MATS + u // 2 + 1))
                act.activation(w_sb[:, half, 0, :, :], w_stage[:, half, :, :], ACT.Copy, scale=WS)\
                   .then_inc(w_high, 1)

            def high_of_next_weights(layer, u):
                act.wait_ge(x_done, layer * X_TILES + (u + 1) * TILES)
                high_of_weights(layer, u + 2)

            high_of_weights(0, 0)
            high_of_weights(0, 1)
            act.wait_ge(counts_stored, 16 * RELS)

            def high_of_hidden(layer, u):
                half = u % 2
                with act.Fori(0, TILES // 2) as tp:
                    for j in range(2):
                        t = 2 * tp + j
                        act.wait_ge(x_done, layer * X_TILES + u * TILES + t + 1)
                        act.activation(h[R, half, 0, ds(t, 1), :].rearrange("p a n -> p (a n)"),
                                       x_bank[j][R, 0:HALF], ACT.Copy, scale=1.0 / WS).then_inc(h_high, 1)

            def high_of_last_relation(layer, half):
                with act.Fori(0, TILES // 2) as tp:
                    for j in range(2):
                        high_of_tile(half, 2 * tp + j, j, (layer + 1) * T_TILES + half * TILES + 2 * tp + j, ACT.Relu)

            def layer_work(layer, last):
                for u in range(2 * MATS):
                    if u >= 2:
                        high_of_hidden(layer, u)
                    if u + 2 < 2 * MATS or not last:
                        high_of_next_weights(layer, u)
                if not last:
                    for half in range(2):
                        high_of_last_relation(layer, half)

            with act.Fori(0, LAYERS - 1) as layer:
                layer_work(layer, False)
            layer_work(LAYERS - 1, True)

            act.wait_ge(ffn_w, 16 * (EXPERTS + 1))
            act.wait_ge(x_done, LAYERS * X_TILES)
            act.activation(w1s[:, 0, :, :], w1_f, ACT.Copy, scale=WS)
            act.activation(encs[:, 0, :, :], enc_f, ACT.Copy, scale=WS).then_inc(ffn_high, 1)
            act.wait_ge(w2_loaded, 16)
            act.activation(w2s[:, 0, :, :], w2_f, ACT.Copy, scale=WS).then_inc(ffn_high, 1)
            root(NORM)
            high_of_normalised(LAYERS * T_TILES)

            minus, total = 1, 2
            act.wait_ge(ffn_small, 80)

            def gelus(c, ks):
                for k in ks:
                    act.wait_ge(hid_done, KH * c + k + 1)
                    if not isinstance(c, int) or c > 0:
                        act.wait_ge(gated_done, KH * (c - 1) + k + 1)
                    act.activation(gel[:, k, :], bank[2 + k % 2][:, 0:TOK], ACT.Gelu, bias=b1s[:, k:k + 1],
                                   scale=1.0 / (XS * WS)).then_inc(gelu_done, 1)

            def token_work(c):
                gelus(c, range(1))
                gelus(c, range(1, KH))
                act.wait_ge(route_step, 7 * c + 3)
                for j in range(2):
                    act.activation(exps[R, j, :], logits[R, j, :], ACT.Exp, bias=route[R, minus, j:j + 1],
                                   accum_out=route[R, total, j:j + 1]).then_inc(exp_done, 1)
                for k in range(KH):
                    act.wait_ge(gated_done, KH * c + k + 1)
                    act.activation(hid[:, 0, k, :], gated[:, k, :], ACT.Copy, scale=XS).then_inc(gated_high, 1)

            act.wait_ge(g_done, LAYERS * G_TILES)
            token_work(0)
            with act.Fori(1, TILES // 2) as c:
                token_work(c)


_INS = ["x", "src", "dst", "etype", "conv_w", "conv_b", "enc_w", "enc_b", "sw_w", "sw_b", "w1", "b1", "w2", "b2"]


def kernel(x, src, dst, edge_type_4, L0_gnn_W1, L0_gnn_root1, L0_gnn_b1, L0_gnn_W2, L0_gnn_root2, L0_gnn_b2,
           L0_gnn_W3, L0_gnn_root3, L0_gnn_b3, L0_ffn_enc_w, L0_ffn_enc_b, L0_ffn_sw_w, L0_ffn_sw_b,
           L0_ffn_w1, L0_ffn_b1, L0_ffn_w2, L0_ffn_b2):
    import numpy as _np
    import concourse.bacc as _bacc
    from concourse import mybir as _mybir
    from concourse.bass_utils import run_bass_kernel_spmd as _run

    conv_w = _np.stack([_np.concatenate([_np.asarray(root)[None], _np.asarray(w)]) for root, w in
                        ((L0_gnn_root1, L0_gnn_W1), (L0_gnn_root2, L0_gnn_W2), (L0_gnn_root3, L0_gnn_W3))])
    conv_b = _np.stack([_np.asarray(b) for b in (L0_gnn_b1, L0_gnn_b2, L0_gnn_b3)])
    given = [x, src, dst, edge_type_4, conv_w, conv_b, L0_ffn_enc_w, L0_ffn_enc_b, L0_ffn_sw_w, L0_ffn_sw_b,
             L0_ffn_w1, L0_ffn_b1, L0_ffn_w2, L0_ffn_b2]

    nc = _bacc.Bacc("TRN2", target_bir_lowering=False, num_devices=1)
    arrays, args = {}, []
    for name, a in zip(_INS, given):
        a = _np.ascontiguousarray(a)
        arrays[f"in_{name}"] = a
        args.append(nc.dram_tensor(f"in_{name}", a.shape, _mybir.dt.from_np(a.dtype), kind="ExternalInput").ap())
    args.append(nc.dram_tensor("out_0", (NODES, D), _mybir.dt.float32, kind="ExternalOutput").ap())
    gnn_ffn(nc, *args)
    r = _run(nc, [arrays], core_ids=[0])
    return r.results[0]["out_0"]
```
